# Optimizing a Trainium2 kernel written in Bass

```python
import numpy as np
import jax
import jax.numpy as jnp

def _softmax(x, axis=-1):
    return jax.nn.softmax(x, axis=axis)

def _gelu(x):
    return jax.nn.gelu(x, approximate=True)

def _silu(x):
    return jax.nn.silu(x)

def _sigmoid(x):
    return jax.nn.sigmoid(x)

def _layernorm(x, axis=-1, eps=1e-05):
    m = jnp.mean(x, axis=axis, keepdims=True)
    v = jnp.var(x, axis=axis, keepdims=True)
    return (x - m) / jnp.sqrt(v + eps)

def _scatter_add(tgt, idx, src, axis=0):
    return tgt.at[idx].add(src)

def _segment_sum(src, seg, n):
    return jax.ops.segment_sum(src, seg, n)
kernel_name = 'mk_dlrm_tower_d1_rec_r8_bb8bbd'

def setup_inputs(seed: int=0):
    np.random.seed(seed)
    _w = jnp.asarray

    def _rec_inputs():
        import jax
        import jax.numpy as jnp
        _tk = jax.random.key(seed)
        ids = jnp.stack([jax.random.randint(jax.random.fold_in(_tk, 200 + f), (512,), 0, v, jnp.int32) for f, v in enumerate([1000, 1250, 1250, 125000, 1250, 12500, 1250, 12500, 12500, 12500, 12500, 1250, 1000, 12500, 12500, 1250, 1250, 1000, 12500, 1000, 1250, 1250, 1000, 1000, 1250, 1000])], axis=1)
        tbl_0 = 0.05 * jax.random.normal(jax.random.fold_in(_tk, 500 + 0), (1000, 128), jnp.float32)
        tbl_1 = 0.05 * jax.random.normal(jax.random.fold_in(_tk, 500 + 1), (1250, 128), jnp.float32)
        tbl_2 = 0.05 * jax.random.normal(jax.random.fold_in(_tk, 500 + 2), (1250, 128), jnp.float32)
        tbl_3 = 0.05 * jax.random.normal(jax.random.fold_in(_tk, 500 + 3), (125000, 128), jnp.float32)
        tbl_4 = 0.05 * jax.random.normal(jax.random.fold_in(_tk, 500 + 4), (1250, 128), jnp.float32)
        tbl_5 = 0.05 * jax.random.normal(jax.random.fold_in(_tk, 500 + 5), (12500, 128), jnp.float32)
        tbl_6 = 0.05 * jax.random.normal(jax.random.fold_in(_tk, 500 + 6), (1250, 128), jnp.float32)
        tbl_7 = 0.05 * jax.random.normal(jax.random.fold_in(_tk, 500 + 7), (12500, 128), jnp.float32)
        tbl_8 = 0.05 * jax.random.normal(jax.random.fold_in(_tk, 500 + 8), (12500, 128), jnp.float32)
        tbl_9 = 0.05 * jax.random.normal(jax.random.fold_in(_tk, 500 + 9), (12500, 128), jnp.float32)
        tbl_10 = 0.05 * jax.random.normal(jax.random.fold_in(_tk, 500 + 10), (12500, 128), jnp.float32)
        tbl_11 = 0.05 * jax.random.normal(jax.random.fold_in(_tk, 500 + 11), (1250, 128), jnp.float32)
        tbl_12 = 0.05 * jax.random.normal(jax.random.fold_in(_tk, 500 + 12), (1000, 128), jnp.float32)
        tbl_13 = 0.05 * jax.random.normal(jax.random.fold_in(_tk, 500 + 13), (12500, 128), jnp.float32)
        tbl_14 = 0.05 * jax.random.normal(jax.random.fold_in(_tk, 500 + 14), (12500, 128), jnp.float32)
        tbl_15 = 0.05 * jax.random.normal(jax.random.fold_in(_tk, 500 + 15), (1250, 128), jnp.float32)
        tbl_16 = 0.05 * jax.random.normal(jax.random.fold_in(_tk, 500 + 16), (1250, 128), jnp.float32)
        tbl_17 = 0.05 * jax.random.normal(jax.random.fold_in(_tk, 500 + 17), (1000, 128), jnp.float32)
        tbl_18 = 0.05 * jax.random.normal(jax.random.fold_in(_tk, 500 + 18), (12500, 128), jnp.float32)
        tbl_19 = 0.05 * jax.random.normal(jax.random.fold_in(_tk, 500 + 19), (1000, 128), jnp.float32)
        tbl_20 = 0.05 * jax.random.normal(jax.random.fold_in(_tk, 500 + 20), (1250, 128), jnp.float32)
        tbl_21 = 0.05 * jax.random.normal(jax.random.fold_in(_tk, 500 + 21), (1250, 128), jnp.float32)
        tbl_22 = 0.05 * jax.random.normal(jax.random.fold_in(_tk, 500 + 22), (1000, 128), jnp.float32)
        tbl_23 = 0.05 * jax.random.normal(jax.random.fold_in(_tk, 500 + 23), (1000, 128), jnp.float32)
        tbl_24 = 0.05 * jax.random.normal(jax.random.fold_in(_tk, 500 + 24), (1250, 128), jnp.float32)
        tbl_25 = 0.05 * jax.random.normal(jax.random.fold_in(_tk, 500 + 25), (1000, 128), jnp.float32)
        _rk = jax.random.fold_in(_tk, 7)
        r_dense_output = -0.000520686 + 1.00062 * jax.random.normal(jax.random.fold_in(_rk, 101), (512, 128), jnp.float32)
        W_top1 = 0.0405887 * jax.random.normal(jax.random.fold_in(_tk, 801), (607, 512), jnp.float32)
        W_top2 = 0.0441942 * jax.random.normal(jax.random.fold_in(_tk, 802), (512, 256), jnp.float32)
        W_top3 = 0.0625 * jax.random.normal(jax.random.fold_in(_tk, 803), (256, 1), jnp.float32)
        b_top1 = jnp.zeros((512,), jnp.float32)
        b_top2 = jnp.zeros((256,), jnp.float32)
        return (r_dense_output, ids, tbl_0, tbl_1, tbl_2, tbl_3, tbl_4, tbl_5, tbl_6, tbl_7, tbl_8, tbl_9, tbl_10, tbl_11, tbl_12, tbl_13, tbl_14, tbl_15, tbl_16, tbl_17, tbl_18, tbl_19, tbl_20, tbl_21, tbl_22, tbl_23, tbl_24, tbl_25, W_top1, b_top1, W_top2, b_top2, W_top3)
    r_dense_output, ids, tbl_0, tbl_1, tbl_2, tbl_3, tbl_4, tbl_5, tbl_6, tbl_7, tbl_8, tbl_9, tbl_10, tbl_11, tbl_12, tbl_13, tbl_14, tbl_15, tbl_16, tbl_17, tbl_18, tbl_19, tbl_20, tbl_21, tbl_22, tbl_23, tbl_24, tbl_25, W_top1, b_top1, W_top2, b_top2, W_top3 = _rec_inputs()

    def _L0_rec_setup():
        import jax, jax.numpy as jnp
        import numpy as np
        B, NUM_SPARSE, D = (2048, 26, 128)
        key = jax.random.key(seed)
        k1, k2 = jax.random.split(key)
        dense_output = jax.random.normal(k1, (B, D), dtype=jnp.float32)
        embeddings = jax.random.normal(k2, (B, NUM_SPARSE, D), dtype=jnp.float32)
        return {'dense_output': dense_output, 'embeddings': embeddings}
    _L0_rec_all = _L0_rec_setup()
    _L0_rec_in = {k: v for k, v in _L0_rec_all.items() if k in ()}
    del _L0_rec_all
    return {'r_dense_output': r_dense_output, 'ids': ids, 'tbl_0': tbl_0, 'tbl_1': tbl_1, 'tbl_2': tbl_2, 'tbl_3': tbl_3, 'tbl_4': tbl_4, 'tbl_5': tbl_5, 'tbl_6': tbl_6, 'tbl_7': tbl_7, 'tbl_8': tbl_8, 'tbl_9': tbl_9, 'tbl_10': tbl_10, 'tbl_11': tbl_11, 'tbl_12': tbl_12, 'tbl_13': tbl_13, 'tbl_14': tbl_14, 'tbl_15': tbl_15, 'tbl_16': tbl_16, 'tbl_17': tbl_17, 'tbl_18': tbl_18, 'tbl_19': tbl_19, 'tbl_20': tbl_20, 'tbl_21': tbl_21, 'tbl_22': tbl_22, 'tbl_23': tbl_23, 'tbl_24': tbl_24, 'tbl_25': tbl_25, 'W_top1': W_top1, 'b_top1': b_top1, 'W_top2': W_top2, 'b_top2': b_top2, 'W_top3': W_top3}

def reference(r_dense_output, ids, tbl_0, tbl_1, tbl_2, tbl_3, tbl_4, tbl_5, tbl_6, tbl_7, tbl_8, tbl_9, tbl_10, tbl_11, tbl_12, tbl_13, tbl_14, tbl_15, tbl_16, tbl_17, tbl_18, tbl_19, tbl_20, tbl_21, tbl_22, tbl_23, tbl_24, tbl_25, W_top1, b_top1, W_top2, b_top2, W_top3):
    import jax
    import jax.numpy as jnp

    def _L0_rec_ref(dense_output, embeddings):
        import jax, jax.numpy as jnp
        import numpy as np
        B, NUM_SPARSE, D = (2048, 26, 128)
        combined = jnp.concatenate([dense_output[:, None, :], embeddings], axis=1)
        interactions = jnp.einsum('bfd,bgd->bfg', combined, combined)
        F = combined.shape[1]
        iu, ju = jnp.triu_indices(F, k=1)
        interactions_flat = interactions[:, iu, ju]
        return jnp.concatenate([dense_output, interactions_flat], axis=1)
    e = jnp.stack([tbl_0[ids[:, 0]], tbl_1[ids[:, 1]], tbl_2[ids[:, 2]], tbl_3[ids[:, 3]], tbl_4[ids[:, 4]], tbl_5[ids[:, 5]], tbl_6[ids[:, 6]], tbl_7[ids[:, 7]], tbl_8[ids[:, 8]], tbl_9[ids[:, 9]], tbl_10[ids[:, 10]], tbl_11[ids[:, 11]], tbl_12[ids[:, 12]], tbl_13[ids[:, 13]], tbl_14[ids[:, 14]], tbl_15[ids[:, 15]], tbl_16[ids[:, 16]], tbl_17[ids[:, 17]], tbl_18[ids[:, 18]], tbl_19[ids[:, 19]], tbl_20[ids[:, 20]], tbl_21[ids[:, 21]], tbl_22[ids[:, 22]], tbl_23[ids[:, 23]], tbl_24[ids[:, 24]], tbl_25[ids[:, 25]]], axis=1)
    z = _L0_rec_ref(r_dense_output, e)
    z = z.reshape(z.shape[0], -1)
    h = jnp.concatenate([z, r_dense_output], axis=1)
    h = jnp.maximum(h @ W_top1 + b_top1, 0.0)
    h = jnp.maximum(h @ W_top2 + b_top2, 0.0)
    y = h @ W_top3
    return y

_drawn_inputs = setup_inputs


def setup_inputs(seed=0):
    import zlib

    import numpy as np

    out = dict(_drawn_inputs(seed))
    spreads = {'b_top1': (0.0, 0.1), 'b_top2': (0.0, 0.1)}
    factors = {}
    for name, (base, spread) in spreads.items():
        noise = np.random.default_rng([zlib.crc32(name.encode()), seed]).standard_normal(out[name].shape)
        drawn = base * np.exp(spread * noise) if base else spread * noise
        out[name] = jnp.asarray(drawn.astype(out[name].dtype))
    for name, factor in factors.items():
        out[name] = (out[name] * factor).astype(out[name].dtype)
    return out
```

```python
import concourse.bass as bass
from concourse import mybir
from contextlib import ExitStack

BATCH, DIM, TABLES = 512, 128, 26
FIELDS = TABLES + 1
PAIRS = FIELDS * (FIELDS - 1) // 2
HID1, HID2 = 512, 256

P = 128
TILES = BATCH // P
PAD = 32
QUADS = P // PAD
SHIFT = FIELDS // 2
BLOCKS = FIELDS - SHIFT
KZ = -(-BLOCKS // QUADS)
M1, M2 = HID1 // P, HID2 // P

ONEHOT = [1, 13, 18, 20, 23, 24, 26]
NOH = len(ONEHOT)
OH_ROWS = 1000
KT = 8
PT = OH_ROWS // KT
STAGED = [4, 5]
IDW = 3

GROUPS = [[2, 3, 4], [5, 6, 7, 8], [9, 10, 11, 12], [14, 15, 16, 17], [19, 21], [22, 25]]
NG = len(GROUPS)
HALF = NG // 2
GATHERED = [f for group in GROUPS for f in group]
FIXED = NOH + 1
PLACE = {f: n for n, f in enumerate(GATHERED)}

WARM_UP = 11
LOOPED = 4
FIRST_GROUPS = {4: (0, 1), 5: (2, 3), 6: (4, 5)}
BANKS = 6
SETS = 4
PER_SET = P // QUADS // SETS
MOVES = 2
PER_MOVE = P // QUADS // MOVES


def pair_row(f, g):
    return DIM + f * (FIELDS - 1) - f * (f - 1) // 2 + g - f - 1


def dlrm_tower(nc, dense, ids, ids_by_table, tables, w1, b1, w2, b2, w3, out):
    fp32, fp32r, i32, bf16, fp16 = (mybir.dt.float32, mybir.dt.float32r, mybir.dt.int32,
                                    mybir.dt.bfloat16, mybir.dt.float16)
    ALU, ACT = mybir.AluOpType, mybir.ActivationFunctionType
    ctx = ExitStack()
    with ctx:
        def sb(name, shape, dt=fp32):
            return ctx.enter_context(nc.sbuf_tensor(name, shape, dt))

        def ps(name, shape):
            return ctx.enter_context(nc.psum_tensor(name, shape, fp32))

        def sem(name):
            return ctx.enter_context(nc.semaphore(name))

        ids_sb = sb("ids_sb", [P, TILES, TABLES], i32)
        dense_sb = sb("dense_sb", [P, TILES, DIM])
        rows = [sb(f"rows{i}", [P, len(GATHERED), DIM]) for i in range(2)]
        ident = sb("ident", [P, P])
        xT = sb("xT", [DIM, BATCH])
        CT = [sb(f"CT{i}", [DIM, P, PAD]) for i in range(2)]
        MG = sb("MG", [P, P // QUADS, BLOCKS])
        behind = sb("behind", [P, SHIFT], i32)
        after = sb("after", [P, SHIFT], i32)
        mask = sb("mask", [P, SHIFT], i32)
        Z = [sb(f"Z{i}", [P, KZ, P]) for i in range(2)]
        w1z = sb("w1z", [P, KZ, HID1])
        w1x = sb("w1x", [P, 2, HID1])
        w1s = sb("w1s", [P, HID1])
        w2_sb = sb("w2_sb", [P, M1, HID2])
        w3_sb = sb("w3_sb", [P, M2])
        b1_sb = sb("b1_sb", [P, M1])
        b2_sb = sb("b2_sb", [P, M2])
        h1 = [sb(f"h1_{i}", [P, M1, P]) for i in range(2)]
        h2 = sb("h2", [P, M2, P])
        y = sb("y", [1, BATCH])

        tab = sb("tab", [PT, NOH, KT * DIM])
        high = sb("high", [PT, 2, KT * DIM], fp32r)
        low = sb("low", [PT, 2, KT * DIM], fp32r)
        idw = sb("idw", [P, IDW, BATCH], i32)
        idh = sb("idh", [PT, IDW, BATCH], fp16)
        zero = sb("zero", [P, 1])
        row_i = sb("row_i", [PT, KT], i32)
        row_h = sb("row_h", [PT, KT, BATCH], fp16)
        staged = sb("staged", [PT, 2, max(STAGED), BATCH], bf16)
        onehot = sb("onehot", [PT, 2, KT, BATCH], fp32r)
        found = sb("found", [DIM, NOH, BATCH])

        pT = [ps(f"pT{i}", [P, 4, P]) for i in range(2)]
        pS = ps("pS", [P, BANKS, 4 * P])
        pG = [pS[:, 2 * i:2 * i + 2, :].rearrange("p b (q c) -> p (b q) c", c=P) for i in range(2)]
        pH = [pS[:, 4 + i, :].rearrange("p (m c) -> p m c", c=P) for i in range(2)]
        pY = pH[0][0:1, 3, :]
        last_banks = [pS[:, i, :].rearrange("p (m c) -> p m c", c=P) for i in range(2)]

        def layer1_bank(t, half):
            return (last_banks if t == TILES - 1 else pH)[half]

        ids_in = sem("ids_in")
        idw_in = [sem(f"idw_in{i}") for i in range(NOH)]
        tab_in = [sem(f"tab_in{i}") for i in range(NOH)]
        dense_in = sem("dense_in")
        wz_in = sem("wz_in")
        wx_in = sem("wx_in")
        w2_in = sem("w2_in")
        small_in = sem("small_in")
        gathered = [[sem(f"gathered{b}_{i}") for i in range(NG)] for b in range(2)]
        w1z_zero = sem("w1z_zero")
        ct_zero = sem("ct_zero")
        ident_zero = sem("ident_zero")
        ident_ready = sem("ident_ready")
        zero_ready = sem("zero_ready")
        row_i_ready = sem("row_i_ready")
        row_h_ready = sem("row_h_ready")
        idh_ready = sem("idh_ready")
        staged_ready = sem("staged_ready")
        direct_ready = sem("direct_ready")
        widened = sem("widened")
        high_ready = sem("high_ready")
        low_ready = sem("low_ready")
        found_ps = sem("found_ps")
        found_ready = sem("found_ready")
        w1s_ready = sem("w1s_ready")
        xT_ps = sem("xT_ps")
        xT_ready = sem("xT_ready")
        transposed = sem("transposed")
        ct_fixed = sem("ct_fixed")
        ct_dve = sem("ct_dve")
        ct_act = sem("ct_act")
        gram = sem("gram")
        behind_ready = sem("behind_ready")
        after_ready = sem("after_ready")
        mask_ready = sem("mask_ready")
        copied = sem("copied")
        merged = sem("merged")
        z_dve = sem("z_dve")
        z_act = sem("z_act")
        h1_ps = sem("h1_ps")
        h1_dve = sem("h1_dve")
        h1_act = sem("h1_act")
        h2_ps = sem("h2_ps")
        h2_dve = sem("h2_dve")
        h2_act = sem("h2_act")
        y_ps = sem("y_ps")
        y_ready = sem("y_ready")
        out_done = sem("out_done")

        SMALL = 3
        WZ = 2 * SHIFT + sum(KZ - (g + 1) // QUADS for g in range(SHIFT))

        block = ctx.enter_context(nc.Block())

        @block.sync
        def _(sp):
            sp.dma_start(ids_sb[:, :, :], ids.rearrange("(t p) f -> p t f", p=P)).then_inc(ids_in, 16)
            for i, f in enumerate(ONEHOT):
                if i >= IDW:
                    sp.wait_ge(idh_ready, i - IDW + 1)
                sp.dma_start(idw[:, i % IDW, :], ids_by_table[f - 1:f, :].to_broadcast([P, BATCH])).then_inc(idw_in[i], 16)
                for part in (slice(0, 120), slice(120, PT)):
                    sp.dma_start(tab[part, i, :], tables[f - 1].rearrange("(p k) d -> p (k d)", k=KT)[part, :]
                                 ).then_inc(tab_in[i], 16)
                if i == 0:
                    sp.dma_start(dense_sb[:, :, :], dense.rearrange("(t p) d -> p t d", p=P)).then_inc(dense_in, 16)
            sp.dma_start(w1x[:, 0, :], w1[0:DIM, :]).then_inc(wx_in, 16)
            sp.dma_start(w1x[:, 1, :], w1[DIM + PAIRS:2 * DIM + PAIRS, :]).then_inc(wx_in, 16)
            sp.dma_start(w2_sb[:, :, :], w2.rearrange("(m p) n -> p m n", p=P)).then_inc(w2_in, 16)
            with nc.allow_non_contiguous_dma(reason="a few hundred bias and weight words"):
                sp.dma_start(b1_sb[:, :], b1.rearrange("(m p) -> p m", p=P)).then_inc(small_in, 16)
                sp.dma_start(b2_sb[:, :], b2.rearrange("(m p) -> p m", p=P)).then_inc(small_in, 16)
                sp.dma_start(w3_sb[:, :], w3.rearrange("(m p) o -> p (m o)", p=P)).then_inc(small_in, 16)
            sp.wait_ge(w1z_zero, 1)
            pieces = []
            for b in range(SHIFT):
                pieces.append((b, 1, b + 1, SHIFT, pair_row(b, b + 1)))
                c = b + SHIFT
                pieces.append((b, 1, c + 1, FIELDS - 1 - c, pair_row(c, c + 1)))
            for g in range(SHIFT):
                b = g + 1
                while b < BLOCKS:
                    n = min(QUADS - b % QUADS, BLOCKS - b)
                    pieces.append((b, n, g, 1, pair_row(g, b + SHIFT)))
                    b += n
            for b, n, g, m, row in pieces:
                p0 = PAD * (b % QUADS) + g
                partitions = slice(p0, p0 + m) if n == 1 else slice(p0, p0 + PAD * (n - 1) + 1, PAD)
                sp.dma_start(w1z[partitions, b // QUADS, :], w1[row:row + n * m, :]).then_inc(wz_in, 16)
            sp.wait_ge(y_ready, TILES)
            sp.dma_start(out.rearrange("b o -> o b"), y[:, :]).then_inc(out_done, 16)
            sp.wait_ge(out_done, 16)

        @block.gpsimd
        def _(pool):
            pool.iota(row_i[:, :], [[1, KT]], base=0, channel_multiplier=KT).then_inc(row_i_ready, 1)
            pool.memset(zero[:, :], 0.0).then_inc(zero_ready, 1)
            pool.memset(ident[:, :], 0.0).then_inc(ident_zero, 1)
            pool.wait_ge(ident_zero, 1)
            pool.affine_select(out=ident[:, :], in_=ident[:, :], compare_op=ALU.not_equal, fill=1.0,
                               base=0, pattern=[[-1, P]], channel_multiplier=1).then_inc(ident_ready, 1)
            pool.wait_ge(ident_ready, 1)
            for s in range(QUADS):
                last = pool.iota(behind[PAD * s:PAD * (s + 1), :], [[-1, SHIFT]], base=0, channel_multiplier=1)
            last.then_inc(behind_ready, 1)
            pool.wait_ge(ids_in, 16)
            for t in range(TILES):
                for i in range(NG):
                    if t >= 2:
                        pool.wait_ge(transposed, NG * (t - 2) + i + 1)
                    for f in GROUPS[i]:
                        pool.indirect_dma_start(
                            out=rows[t % 2][:, PLACE[f], :], out_offset=None, in_=tables[f - 1][:, :],
                            in_offset=bass.IndirectOffsetOnAxis(ap=ids_sb[:, t, f - 1:f], axis=0)
                        ).then_inc(gathered[t % 2][i], 16)

        def table_columns(r, s, first, n):
            return pG[r % 2][PAD * s:PAD * (s + 1), :, s * FIELDS + first:s * FIELDS + first + n]

        def merged_columns(r, s, n):
            return MG[PAD * s:PAD * (s + 1), r * PER_SET:(r + 1) * PER_SET, 0:n]

        def move_merged(copy, samples, t, part, done):
            for s in samples:
                for j in range(QUADS):
                    n = (BLOCKS - j + QUADS - 1) // QUADS
                    q0 = part * PER_MOVE
                    b = q0 * QUADS + s
                    src = MG[PAD * s:PAD * (s + 1), q0:q0 + PER_MOVE, j:j + QUADS * (n - 1) + 1:QUADS]
                    dst = Z[t % 2][PAD * j:PAD * (j + 1), 0:n, b:b + QUADS * (PER_MOVE - 1) + 1:QUADS]
                    last = copy(dst.rearrange("p k q -> p q k"), src)
            last.then_inc(done, 1)

        def evacuate_group(copy, t, i, done):
            fields = GROUPS[i]
            columns = CT[t % 2][:, :, fields[0]:fields[-1] + 1:fields[1] - fields[0]]
            copy(columns.rearrange("p b f -> p f b"), pT[i % 2][:, 0:len(fields), :]).then_inc(done, 1)

        @block.tensor
        def _(pe):
            def transposes(t, i):
                pe.wait_ge(gathered[t % 2][i], 16 * len(GROUPS[i]) * (t // 2 + 1))
                before = HALF * t + i // 2
                if before:
                    pe.wait_ge(ct_act if i % 2 else ct_dve, before)
                for n, f in enumerate(GROUPS[i]):
                    last = nc.tensor.transpose(pT[i % 2][:, n, :], rows[t % 2][:, PLACE[f], :], ident[:, :])
                last.then_inc(transposed, 1)

            pe.wait_ge(ident_ready, 1)
            for _ in range(WARM_UP):
                nc.tensor.matmul(pT[0][:, 0, :], ident[:, :], ident[:, :], start=True, stop=True)

            pe.wait_ge(dense_in, 16)
            for t in range(TILES):
                last = nc.tensor.transpose(pT[1][:, t, :], dense_sb[:, t, :], ident[:, :])
            last.then_inc(xT_ps, 1)

            def look_up(i, odd, found_bank):
                for part, ready, ks in ((high, direct_ready, range(STAGED[odd], KT)), (high, widened, range(STAGED[odd])),
                                        (low, low_ready, range(KT))):
                    pe.wait_ge(ready, i + 1)
                    if ready is direct_ready:
                        pe.wait_ge(high_ready, i + 1)
                    for k in ks:
                        last = nc.tensor.matmul(found_bank, part[:, odd, k * DIM:(k + 1) * DIM], onehot[:, odd, k, :],
                                                start=(part is high and k == STAGED[odd]), stop=(part is low and k == KT - 1))
                last.then_inc(found_ps, 1)

            with pe.Fori(0, LOOPED // 2) as pair:
                for odd in range(2):
                    look_up(2 * pair + odd, odd, pS[:, odd::2, :][:, bass.ds(pair, 1), :].rearrange("p i b -> p (i b)"))
            pe.wait_ge(xT_ready, 1)
            for i in range(LOOPED, NOH):
                for g in FIRST_GROUPS.get(i, ()):
                    transposes(0, g)
                if i >= BANKS:
                    pe.wait_ge(found_ready, i - BANKS + 1)
                look_up(i, i % 2, pS[:, i % BANKS, :])

            def product_set(t, r):
                if r >= 2:
                    pe.wait_ge(merged, SETS * t + r - 1)
                elif t >= 1:
                    pe.wait_ge(merged, SETS * (t - 1) + r + 3)
                for q in range(PER_SET):
                    four = slice(QUADS * (r * PER_SET + q), QUADS * (r * PER_SET + q + 1))
                    last = nc.tensor.matmul(
                        pG[r % 2][:, q, 0:QUADS * FIELDS].rearrange("p (s f) -> p s f", s=QUADS),
                        CT[t % 2][:, four, :].rearrange("p s f -> p (s f)"), CT[t % 2][:, four, 0:FIELDS],
                        start=True, stop=True)
                last.then_inc(gram, 1)

            def layer1(t, half, bank):
                if t == 0:
                    pe.wait_ge(wz_in, 16 * WZ)
                    pe.wait_ge(w1s_ready, 1)
                pe.wait_ge(z_dve, MOVES * (t + 1))
                pe.wait_ge(z_act, MOVES * (t + 1))
                if t >= 1 and bank is pH[0]:
                    pe.wait_ge(y_ready, t)
                for m in (2 * half, 2 * half + 1):
                    acc, cols = bank[:, m % 2, :], slice(m * P, (m + 1) * P)
                    nc.tensor.matmul(acc, w1s[:, cols], xT[:, t * P:(t + 1) * P], start=True, stop=False)
                    for k in range(KZ):
                        used = PAD * min(BLOCKS - QUADS * k, QUADS)
                        last = nc.tensor.matmul(acc, w1z[0:used, k, cols], Z[t % 2][0:used, k, :],
                                                start=False, stop=(k == KZ - 1))
                last.then_inc(h1_ps, 1)

            def layer2(t):
                if t == 0:
                    pe.wait_ge(w2_in, 16)
                    pe.wait_ge(small_in, 16 * SMALL)
                if t < TILES - 1:
                    pe.wait_ge(h1_act, t + 1)
                for k0, ready in ((0, h1_dve), (2, h1_act)):
                    pe.wait_ge(ready, t + 1)
                    for m in range(M2):
                        for k in (k0, k0 + 1):
                            last = nc.tensor.matmul(pH[m][:, 2, :], w2_sb[:, k, m * P:(m + 1) * P], h1[t % 2][:, k, :],
                                                    start=(k == 0), stop=(k == M1 - 1))
                        if k0:
                            last.then_inc(h2_ps, 1)

            def layer3(t):
                for k, ready in enumerate((h2_dve, h2_act)):
                    pe.wait_ge(ready, t + 1)
                    last = nc.tensor.matmul(pY, w3_sb[:, k:k + 1], h2[:, k, :], start=(k == 0), stop=(k == M2 - 1))
                last.then_inc(y_ps, 1)

            for t in range(TILES):
                def next_tile(*groups):
                    if t + 1 < TILES:
                        for i in groups:
                            transposes(t + 1, i)

                pe.wait_ge(ct_fixed, FIXED * (t + 1))
                pe.wait_ge(ct_dve, HALF * (t + 1))
                pe.wait_ge(ct_act, HALF * (t + 1))
                if t == 0:
                    pe.wait_ge(found_ready, NOH)
                product_set(t, 0)
                if 2 <= t < TILES - 1:
                    layer3(t - 2)
                product_set(t, 1)
                next_tile(0)
                if 1 <= t < TILES - 1:
                    layer1(t - 1, 0, pH[0])
                product_set(t, 2)
                if t == TILES - 1:
                    break
                next_tile(1)
                if t >= 1:
                    layer1(t - 1, 1, pH[1])
                next_tile(2)
                product_set(t, 3)
                if t < TILES - 2:
                    next_tile(3, 4, 5)
                    if t >= 1:
                        layer2(t - 1)
                else:
                    next_tile(3)
                    layer2(t - 1)
                    next_tile(4)
                    layer3(t - 1)
                    layer1(t, 0, pH[0])
                    next_tile(5)
                    layer1(t, 1, pH[1])
            product_set(TILES - 1, 3)
            layer2(TILES - 2)
            layer1(TILES - 1, 0, last_banks[0])
            layer3(TILES - 2)
            layer1(TILES - 1, 1, last_banks[1])
            pe.wait_ge(y_ready, TILES - 1)
            layer2(TILES - 1)
            layer3(TILES - 1)

        def row_numbers(copy, ks):
            return copy(row_h[:, ks, :], row_i[:, ks, None].to_broadcast([PT, ks.stop - ks.start, BATCH]))

        @block.scalar
        def _(act):
            def copy(dst, src):
                return nc.scalar.copy(dst, src)

            def fixed_field(t, f, source):
                column = CT[t % 2][:, :, f:f + 1].rearrange("p b f -> p (b f)")
                copy(column, source[:, t * P:(t + 1) * P]).then_inc(ct_fixed, 1)

            def fixed_fields(t):
                if t == 1:
                    act.wait_ge(ct_zero, 2)
                if t >= 2:
                    act.wait_ge(gram, SETS * (t - 1))
                fixed_field(t, 0, xT)
                for i, f in enumerate(ONEHOT):
                    fixed_field(t, f, found[:, i, :])

            def group(t, i):
                act.wait_ge(transposed, NG * t + i + 1)
                evacuate_group(copy, t, i, ct_act)

            def base_columns(t, r):
                act.wait_ge(gram, SETS * t + r + 1)
                if t >= 1 and r % (SETS // MOVES) == 0:
                    act.wait_ge(z_dve, MOVES * (t - 1) + r // (SETS // MOVES) + 1)
                for s in range(QUADS):
                    last = copy(merged_columns(r, s, BLOCKS), table_columns(r, s, SHIFT, BLOCKS))
                last.then_inc(copied, 1)

            def move(t, part):
                act.wait_ge(merged, SETS * t + (part + 1) * (SETS // MOVES))
                move_merged(copy, (2, 3), t, part, z_act)

            def hidden1(t):
                if t == 0:
                    act.wait_ge(small_in, 16 * SMALL)
                act.wait_ge(h1_ps, 2 * (t + 1))
                for m in (2, 3):
                    last = nc.scalar.activation(h1[t % 2][:, m, :], layer1_bank(t, 1)[:, m % 2, :], ACT.Relu, bias=b1_sb[:, m:m + 1])
                last.then_inc(h1_act, 1)

            def hidden2(t):
                act.wait_ge(h2_ps, M2 * (t + 1))
                nc.scalar.activation(h2[:, 1, :], pH[1][:, 2, :], ACT.Relu, bias=b2_sb[:, 1:2]).then_inc(h2_act, 1)

            act.wait_ge(row_i_ready, 1)
            row_numbers(copy, slice(0, KT // 2)).then_inc(row_h_ready, 1)
            def convert_ids(i):
                act.wait_ge(idw_in[i], 16)
                if i >= IDW:
                    act.wait_ge(direct_ready, i - IDW + 1)
                copy(idh[:, i % IDW, :], idw[0:PT, i % IDW, :]).then_inc(idh_ready, 1)

            def round_table(i):
                act.wait_ge(tab_in[i], 32)
                if i >= 2:
                    act.wait_ge(found_ps, i - 1)
                copy(high[:, i % 2, :], tab[:, i, :]).then_inc(high_ready, 1)

            def widen(i):
                act.wait_ge(staged_ready, i + 1)
                if i >= 2:
                    act.wait_ge(found_ps, i - 1)
                n = STAGED[i % 2]
                copy(onehot[:, i % 2, 0:n, :], staged[:, i % 2, 0:n, :]).then_inc(widened, 1)

            def rows_found(i):
                act.wait_ge(found_ps, i + 1)
                copy(found[:, i, :], pS[:, i % BANKS, :]).then_inc(found_ready, 1)

            def found_fields(i):
                act.wait_ge(found_ready, i + 1)
                fixed_field(0, ONEHOT[i], found[:, i, :])

            convert_ids(0)
            act.wait_ge(zero_ready, 1)
            copy(w1z[:, :, :], zero[:, None, :].to_broadcast([P, KZ, HID1])).then_inc(w1z_zero, 1)
            for i in range(NOH):
                if i == 0:
                    widen(i)
                if i >= 2:
                    rows_found(i - 2)
                round_table(i)
                if i + 1 < NOH:
                    convert_ids(i + 1)
                if i > 0:
                    widen(i)
                if i == 0:
                    act.wait_ge(xT_ps, 1)
                    copy(xT[:, :], pT[1][:, :, :].rearrange("p t b -> p (t b)")).then_inc(xT_ready, 1)
                if i == 1:
                    act.wait_ge(ct_zero, 1)
                    act.wait_ge(xT_ready, 1)
                    fixed_field(0, 0, xT)
                if i >= 2:
                    found_fields(i - 2)
                for g in FIRST_GROUPS.get(i, ()):
                    if g % 2:
                        group(0, g)
            for i in range(NOH - 2, NOH):
                rows_found(i)
                found_fields(i)
            for t in range(TILES):
                base_columns(t, 0)
                base_columns(t, 1)
                if t + 1 < TILES:
                    fixed_fields(t + 1)
                move(t, 0)
                base_columns(t, 2)
                if t + 1 < TILES:
                    group(t + 1, 1)
                if t == TILES - 1:
                    break
                if t >= 1:
                    hidden1(t - 1)
                base_columns(t, 3)
                group(t + 1, 3)
                if t < TILES - 2:
                    group(t + 1, 5)
                move(t, 1)
                if t >= 1:
                    hidden2(t - 1)
                if t == TILES - 2:
                    group(t + 1, 5)
                    hidden1(t)
            base_columns(TILES - 1, 3)
            move(TILES - 1, 1)
            hidden2(TILES - 2)
            hidden1(TILES - 1)
            hidden2(TILES - 1)

        @block.vector
        def _(dve):
            def copy(dst, src):
                return nc.vector.tensor_copy(dst, src)

            def group(t, i):
                dve.wait_ge(transposed, NG * t + i + 1)
                evacuate_group(copy, t, i, ct_dve)

            def merge(t, r):
                dve.wait_ge(copied, SETS * t + r + 1)
                for s in range(QUADS):
                    out_cols = merged_columns(r, s, SHIFT)
                    keep = mask[PAD * s:PAD * (s + 1), None, :].to_broadcast(list(out_cols.shape))
                    last = nc.vector.copy_predicated(out_cols, keep, table_columns(r, s, 0, SHIFT))
                last.then_inc(merged, 1)

            def move(t, part):
                dve.wait_ge(merged, SETS * t + (part + 1) * (SETS // MOVES))
                move_merged(copy, (0, 1), t, part, z_dve)

            def hidden1(t):
                if t == 0:
                    dve.wait_ge(small_in, 16 * SMALL)
                dve.wait_ge(h1_ps, 2 * t + 1)
                for m in (0, 1):
                    last = nc.vector.tensor_scalar(h1[t % 2][:, m, :], layer1_bank(t, 0)[:, m, :], b1_sb[:, m:m + 1], 0.0,
                                                   ALU.add, ALU.max)
                last.then_inc(h1_dve, 1)

            def hidden2(t):
                dve.wait_ge(h2_ps, M2 * t + 1)
                nc.vector.tensor_scalar(h2[:, 0, :], pH[0][:, 2, :], b2_sb[:, 0:1], 0.0,
                                        ALU.add, ALU.max).then_inc(h2_dve, 1)

            def result(t):
                dve.wait_ge(y_ps, t + 1)
                nc.vector.tensor_copy(y[:, bass.ds(t * P, P)], pY).then_inc(y_ready, 1)

            def one_hot(out, i, ks):
                return nc.vector.tensor_tensor(out, row_h[:, ks, :],
                                               idh[:, i % IDW, None, :].to_broadcast([PT, ks.stop - ks.start, BATCH]), ALU.is_equal)

            dve.wait_ge(row_i_ready, 1)
            row_numbers(copy, slice(KT // 2, KT)).then_inc(row_h_ready, 1)
            nc.vector.memset(CT[0][:, :, FIELDS:PAD], 0.0).then_inc(ct_zero, 1)
            dve.wait_ge(row_h_ready, 2)
            for i in range(NOH):
                dve.wait_ge(idh_ready, i + 1)
                if i >= 2:
                    dve.wait_ge(widened, i - 1)
                n = STAGED[i % 2]
                one_hot(staged[:, i % 2, 0:n, :], i, slice(0, n)).then_inc(staged_ready, 1)
                if i >= 2:
                    dve.wait_ge(found_ps, i - 1)
                one_hot(onehot[:, i % 2, n:KT, :], i, slice(n, KT)).then_inc(direct_ready, 1)
                dve.wait_ge(tab_in[i], 32)
                dve.wait_ge(high_ready, i + 1)
                nc.vector.tensor_tensor(low[:, i % 2, :], tab[:, i, :], high[:, i % 2, :].bitcast(fp32),
                                        ALU.subtract).then_inc(low_ready, 1)
                for g in FIRST_GROUPS.get(i, ()):
                    if g % 2 == 0:
                        group(0, g)
            dve.wait_ge(behind_ready, 1)
            nc.vector.tensor_scalar(after[:, :], behind[:, :], 1, None, ALU.is_ge).then_inc(after_ready, 1)
            dve.wait_ge(after_ready, 1)
            nc.vector.scalar_tensor_tensor(mask[:, :], behind[:, :], SHIFT, after[:, :],
                                           ALU.is_le, ALU.mult).then_inc(mask_ready, 1)
            nc.vector.memset(CT[1][:, :, FIELDS:PAD], 0.0).then_inc(ct_zero, 1)
            dve.wait_ge(wx_in, 32)
            nc.vector.tensor_tensor(w1s[:, :], w1x[:, 0, :], w1x[:, 1, :], ALU.add).then_inc(w1s_ready, 1)
            dve.wait_ge(mask_ready, 1)
            for t in range(TILES):
                merge(t, 0)
                if 2 <= t < TILES - 1:
                    result(t - 2)
                merge(t, 1)
                move(t, 0)
                if t + 1 < TILES:
                    group(t + 1, 0)
                if 1 <= t < TILES - 1:
                    hidden1(t - 1)
                merge(t, 2)
                if t + 1 < TILES:
                    group(t + 1, 2)
                merge(t, 3)
                if t == TILES - 1:
                    break
                if t < TILES - 2:
                    group(t + 1, 4)
                    move(t, 1)
                    if t >= 1:
                        hidden2(t - 1)
                else:
                    move(t, 1)
                    hidden2(t - 1)
                    group(t + 1, 4)
                    result(t - 1)
                    hidden1(t)
            move(TILES - 1, 1)
            hidden2(TILES - 2)
            hidden1(TILES - 1)
            result(TILES - 2)
            hidden2(TILES - 1)
            result(TILES - 1)



_INS = (["r_dense_output", "ids", "ids_by_table"] + [f"tbl_{i}" for i in range(TABLES)]
        + ["W_top1", "b_top1", "W_top2", "b_top2", "W_top3"])


def kernel(**inputs):
    import numpy as _np
    import concourse.bacc as _bacc
    from concourse import mybir as _mybir
    from concourse.bass_utils import run_bass_kernel_spmd as _run

    nc = _bacc.Bacc("TRN2", target_bir_lowering=False, num_devices=1)
    arrays, args = {}, []
    inputs["ids_by_table"] = _np.asarray(inputs["ids"]).T
    for name in _INS:
        a = _np.ascontiguousarray(inputs[name])
        arrays[f"in_{name}_dram"] = a
        args.append(nc.dram_tensor(f"in_{name}_dram", a.shape, _mybir.dt.from_np(a.dtype), kind="ExternalInput").ap())
    out = nc.dram_tensor("out_0_dram", (BATCH, 1), _mybir.dt.float32, kind="ExternalOutput").ap()
    dlrm_tower(nc, *args[:3], args[3:3 + TABLES], *args[3 + TABLES:], out)
    r = _run(nc, [arrays], core_ids=[0])
    return r.results[0]["out_0_dram"]
```

```python
import concourse.bass as bass
from concourse import mybir
from contextlib import ExitStack

BATCH, DIM, TABLES = 512, 128, 26
FIELDS = TABLES + 1
PAIRS = FIELDS * (FIELDS - 1) // 2
HID1, HID2 = 512, 256

P = 128
TILES = BATCH // P
PAD = 32
QUADS = P // PAD
SHIFT = FIELDS // 2
BLOCKS = FIELDS - SHIFT
KZ = -(-BLOCKS // QUADS)
M1, M2 = HID1 // P, HID2 // P

ONEHOT = [1, 13, 18, 20, 23, 24, 26]
NOH = len(ONEHOT)
OH_ROWS = 1000
KT = 8
PT = OH_ROWS // KT
STAGED = [4, 5]
EARLY = 16
IDW = 3

GROUPS = [[2, 3, 4], [5, 6, 7, 8], [9, 10, 11, 12], [14, 15, 16, 17], [19, 21], [22, 25]]
NG = len(GROUPS)
HALF = NG // 2
GATHERED = [f for group in GROUPS for f in group]
FIXED = NOH + 1
PLACE = {f: n for n, f in enumerate(GATHERED)}

WARM_UP = 11
LOOPED = 4
FIRST_GROUPS = {4: (0, 1), 5: (2, 3), 6: (4, 5)}
GRAM_ROWS = P - (PAD - FIELDS)
BANKS = 6
SETS = 4
PER_SET = P // QUADS // SETS
HALVES = ((2, 3), (0, 1))
MOVES = 2
PER_MOVE = P // QUADS // MOVES


def pair_row(f, g):
    return DIM + f * (FIELDS - 1) - f * (f - 1) // 2 + g - f - 1


def dlrm_tower(nc, dense, ids, ids_by_table, tables, w1, b1, w2, b2, w3, out):
    fp32, fp32r, i32, bf16, fp16 = (mybir.dt.float32, mybir.dt.float32r, mybir.dt.int32,
                                    mybir.dt.bfloat16, mybir.dt.float16)
    ALU, ACT = mybir.AluOpType, mybir.ActivationFunctionType
    ctx = ExitStack()
    with ctx:
        def sb(name, shape, dt=fp32):
            return ctx.enter_context(nc.sbuf_tensor(name, shape, dt))

        def ps(name, shape):
            return ctx.enter_context(nc.psum_tensor(name, shape, fp32))

        def sem(name):
            return ctx.enter_context(nc.semaphore(name))

        ids_sb = sb("ids_sb", [P, TILES, TABLES], i32)
        dense_sb = sb("dense_sb", [P, TILES, DIM])
        rows = [sb(f"rows{i}", [P, len(GATHERED), DIM]) for i in range(2)]
        ident = sb("ident", [P, P])
        xT = sb("xT", [DIM, BATCH])
        CT = [sb(f"CT{i}", [DIM, P, PAD]) for i in range(2)]
        MG = sb("MG", [P, P // QUADS, BLOCKS])
        behind = sb("behind", [P, SHIFT], i32)
        after = sb("after", [P, SHIFT], i32)
        mask = sb("mask", [P, SHIFT], i32)
        Z = [sb(f"Z{i}", [P, KZ, P]) for i in range(2)]
        w1z = sb("w1z", [P, KZ, HID1])
        w1x = sb("w1x", [P, 2, HID1])
        w1s = sb("w1s", [P, HID1])
        w2_sb = sb("w2_sb", [P, M1, HID2])
        w3_sb = sb("w3_sb", [P, M2])
        b1_sb = sb("b1_sb", [P, M1])
        b2_sb = sb("b2_sb", [P, M2])
        h1 = [sb(f"h1_{i}", [P, M1, P]) for i in range(2)]
        h2 = sb("h2", [P, M2, P])
        y = sb("y", [1, BATCH])

        tab = sb("tab", [PT, NOH, KT * DIM])
        high = sb("high", [PT, 2, KT * DIM], fp32r)
        low = sb("low", [PT, 2, KT * DIM], fp32r)
        idw = sb("idw", [P, IDW, BATCH], i32)
        idh = sb("idh", [PT, IDW, BATCH], fp16)
        zero = sb("zero", [P, 1])
        row_i = sb("row_i", [PT, KT], i32)
        row_h = sb("row_h", [PT, KT, BATCH], fp16)
        staged = sb("staged", [PT, 2, max(STAGED), BATCH], bf16)
        onehot = sb("onehot", [PT, 2, KT, BATCH], fp32r)
        found = sb("found", [DIM, NOH, BATCH])

        pT = [ps(f"pT{i}", [P, 4, P]) for i in range(2)]
        pS = ps("pS", [P, BANKS, 4 * P])
        pG = [pS[:, 2 * i:2 * i + 2, :].rearrange("p b (q c) -> p (b q) c", c=P) for i in range(2)]
        pH = [pS[:, 4 + i, :].rearrange("p (m c) -> p m c", c=P) for i in range(2)]
        pY = pH[0][0:1, 3, :]
        last_blocks = [pS[:, 0, 0:P], pT[0][:, 0, :], pS[:, 1, 0:P], pT[1][:, 0, :]]

        def layer1_block(t, m):
            return last_blocks[m] if t == TILES - 1 else pH[m // 2][:, m % 2, :]

        def found_bank(i):
            return pS[:, i if i < BANKS else i - 2, :]

        def halves_done(t, half):
            return 2 * t + 1 + (half if t != TILES - 2 else 1 - half)

        ids_in = sem("ids_in")
        idw_in = [sem(f"idw_in{i}") for i in range(NOH)]
        tab_in = [sem(f"tab_in{i}") for i in range(NOH)]
        dense_in = sem("dense_in")
        wz_in = sem("wz_in")
        wx_in = sem("wx_in")
        w2_in = sem("w2_in")
        small_in = sem("small_in")
        gathered = [[sem(f"gathered{b}_{i}") for i in range(NG)] for b in range(2)]
        w1z_zero = sem("w1z_zero")
        ct_zero = sem("ct_zero")
        ident_zero = sem("ident_zero")
        ident_ready = sem("ident_ready")
        zero_ready = sem("zero_ready")
        row_i_ready = sem("row_i_ready")
        row_h_ready = sem("row_h_ready")
        idh_ready = sem("idh_ready")
        staged_ready = sem("staged_ready")
        direct_ready = sem("direct_ready")
        widened = sem("widened")
        high_ready = sem("high_ready")
        low_ready = sem("low_ready")
        found_ps = sem("found_ps")
        found_ready = sem("found_ready")
        w1s_ready = sem("w1s_ready")
        xT_ps = sem("xT_ps")
        xT_ready = sem("xT_ready")
        transposed = sem("transposed")
        ct_fixed = sem("ct_fixed")
        ct_dve = sem("ct_dve")
        ct_act = sem("ct_act")
        gram = sem("gram")
        behind_ready = sem("behind_ready")
        after_ready = sem("after_ready")
        mask_ready = sem("mask_ready")
        copied = sem("copied")
        merged = sem("merged")
        z_zero = sem("z_zero")
        z_dve = sem("z_dve")
        z_act = sem("z_act")
        h1_ps = sem("h1_ps")
        h1_dve = sem("h1_dve")
        h1_act = sem("h1_act")
        h2_ps = sem("h2_ps")
        h2_dve = sem("h2_dve")
        h2_act = sem("h2_act")
        y_ps = sem("y_ps")
        y_ready = sem("y_ready")
        out_done = sem("out_done")

        SMALL = 3
        WZ = 2 * SHIFT + sum(KZ - (g + 1) // QUADS for g in range(SHIFT))

        block = ctx.enter_context(nc.Block())

        @block.sync
        def _(sp):
            pieces = []
            for b in range(SHIFT):
                pieces.append((b, 1, b + 1, SHIFT, pair_row(b, b + 1)))
                c = b + SHIFT
                pieces.append((b, 1, c + 1, FIELDS - 1 - c, pair_row(c, c + 1)))
            for g in range(SHIFT):
                b = g + 1
                while b < BLOCKS:
                    n = min(QUADS - b % QUADS, BLOCKS - b)
                    pieces.append((b, n, g, 1, pair_row(g, b + SHIFT)))
                    b += n

            def load_w1z(pieces):
                for b, n, g, m, row in pieces:
                    p0 = PAD * (b % QUADS) + g
                    partitions = slice(p0, p0 + m) if n == 1 else slice(p0, p0 + PAD * (n - 1) + 1, PAD)
                    sp.dma_start(w1z[partitions, b // QUADS, :], w1[row:row + n * m, :]).then_inc(wz_in, 16)

            sp.dma_start(ids_sb[:, :, :], ids.rearrange("(t p) f -> p t f", p=P)).then_inc(ids_in, 16)
            for i, f in enumerate(ONEHOT):
                if i == NOH - 2:
                    sp.wait_ge(w1z_zero, 1)
                    load_w1z(pieces[:EARLY])
                if i >= IDW:
                    sp.wait_ge(idh_ready, i - IDW + 1)
                sp.dma_start(idw[:, i % IDW, :], ids_by_table[f - 1:f, :].to_broadcast([P, BATCH])).then_inc(idw_in[i], 16)
                for part in (slice(0, 120), slice(120, PT)):
                    sp.dma_start(tab[part, i, :], tables[f - 1].rearrange("(p k) d -> p (k d)", k=KT)[part, :]
                                 ).then_inc(tab_in[i], 16)
                if i == 0:
                    sp.dma_start(dense_sb[:, :, :], dense.rearrange("(t p) d -> p t d", p=P)).then_inc(dense_in, 16)
            sp.dma_start(w1x[:, 0, :], w1[0:DIM, :]).then_inc(wx_in, 16)
            sp.dma_start(w1x[:, 1, :], w1[DIM + PAIRS:2 * DIM + PAIRS, :]).then_inc(wx_in, 16)
            load_w1z(pieces[EARLY:])
            sp.dma_start(w2_sb[:, :, :], w2.rearrange("(m p) n -> p m n", p=P)).then_inc(w2_in, 16)
            with nc.allow_non_contiguous_dma(reason="a few hundred bias and weight words"):
                sp.dma_start(b1_sb[:, :], b1.rearrange("(m p) -> p m", p=P)).then_inc(small_in, 16)
                sp.dma_start(b2_sb[:, :], b2.rearrange("(m p) -> p m", p=P)).then_inc(small_in, 16)
                sp.dma_start(w3_sb[:, :], w3.rearrange("(m p) o -> p (m o)", p=P)).then_inc(small_in, 16)
            sp.wait_ge(y_ready, TILES)
            sp.dma_start(out.rearrange("b o -> o b"), y[:, :]).then_inc(out_done, 16)
            sp.wait_ge(out_done, 16)

        @block.gpsimd
        def _(pool):
            pool.iota(row_i[:, :], [[1, KT]], base=0, channel_multiplier=KT).then_inc(row_i_ready, 1)
            pool.memset(zero[:, :], 0.0).then_inc(zero_ready, 1)
            pool.memset(ident[:, :], 0.0).then_inc(ident_zero, 1)
            pool.wait_ge(ident_zero, 1)
            pool.affine_select(out=ident[:, :], in_=ident[:, :], compare_op=ALU.not_equal, fill=1.0,
                               base=0, pattern=[[-1, P]], channel_multiplier=1).then_inc(ident_ready, 1)
            pool.wait_ge(ident_ready, 1)
            for s in range(QUADS):
                last = pool.iota(behind[PAD * s:PAD * (s + 1), :], [[-1, SHIFT]], base=0, channel_multiplier=1)
            last.then_inc(behind_ready, 1)
            pool.wait_ge(behind_ready, 1)
            for i in range(2):
                pool.memset(Z[i][:, :, :], 0.0).then_inc(z_zero, 1)
            pool.wait_ge(ids_in, 16)
            for t in range(TILES):
                for i in range(NG):
                    if t >= 2:
                        pool.wait_ge(transposed, NG * (t - 2) + i + 1)
                    for f in GROUPS[i]:
                        pool.indirect_dma_start(
                            out=rows[t % 2][:, PLACE[f], :], out_offset=None, in_=tables[f - 1][:, :],
                            in_offset=bass.IndirectOffsetOnAxis(ap=ids_sb[:, t, f - 1:f], axis=0)
                        ).then_inc(gathered[t % 2][i], 16)

        def used_rows(s):
            return slice(PAD * s, min(PAD * (s + 1), GRAM_ROWS))

        def table_columns(r, s, first, n):
            return pG[r % 2][used_rows(s), :, s * FIELDS + first:s * FIELDS + first + n]

        def merged_columns(r, s, n):
            return MG[used_rows(s), r * PER_SET:(r + 1) * PER_SET, 0:n]

        def move_merged(copy, samples, t, part, done):
            for s in samples:
                for j in range(QUADS):
                    n = (BLOCKS - j + QUADS - 1) // QUADS
                    q0 = part * PER_MOVE
                    b = q0 * QUADS + s
                    src = MG[used_rows(s), q0:q0 + PER_MOVE, j:j + QUADS * (n - 1) + 1:QUADS]
                    dst = Z[t % 2][PAD * j:PAD * j + src.shape[0], 0:n, b:b + QUADS * (PER_MOVE - 1) + 1:QUADS]
                    last = copy(dst.rearrange("p k q -> p q k"), src)
            last.then_inc(done, 1)

        def evacuate_group(copy, t, i, done):
            fields = GROUPS[i]
            columns = CT[t % 2][:, :, fields[0]:fields[-1] + 1:fields[1] - fields[0]]
            copy(columns.rearrange("p b f -> p f b"), pT[i % 2][:, 0:len(fields), :]).then_inc(done, 1)

        @block.tensor
        def _(pe):
            def transposes(t, i):
                pe.wait_ge(gathered[t % 2][i], 16 * len(GROUPS[i]) * (t // 2 + 1))
                before = HALF * t + i // 2
                if before:
                    pe.wait_ge(ct_act if i % 2 else ct_dve, before)
                for n, f in enumerate(GROUPS[i]):
                    last = nc.tensor.transpose(pT[i % 2][:, n, :], rows[t % 2][:, PLACE[f], :], ident[:, :])
                last.then_inc(transposed, 1)

            pe.wait_ge(ident_ready, 1)
            for _ in range(WARM_UP):
                nc.tensor.matmul(pT[0][:, 0, :], ident[:, :], ident[:, :], start=True, stop=True)

            pe.wait_ge(dense_in, 16)
            for t in range(TILES):
                last = nc.tensor.transpose(pT[1][:, t, :], dense_sb[:, t, :], ident[:, :])
            last.then_inc(xT_ps, 1)

            def look_up(i, odd, bank):
                for part, ready, ks in ((high, direct_ready, range(STAGED[odd], KT)), (high, widened, range(STAGED[odd])),
                                        (low, low_ready, range(KT))):
                    pe.wait_ge(ready, i + 1)
                    if ready is direct_ready:
                        pe.wait_ge(high_ready, i + 1)
                    for k in ks:
                        last = nc.tensor.matmul(bank, part[:, odd, k * DIM:(k + 1) * DIM], onehot[:, odd, k, :],
                                                start=(part is high and k == STAGED[odd]), stop=(part is low and k == KT - 1))
                last.then_inc(found_ps, 1)

            with pe.Fori(0, LOOPED // 2) as pair:
                for odd in range(2):
                    look_up(2 * pair + odd, odd, pS[:, odd::2, :][:, bass.ds(pair, 1), :].rearrange("p i b -> p (i b)"))
            pe.wait_ge(xT_ready, 1)
            for i in range(LOOPED, NOH):
                for g in FIRST_GROUPS.get(i, ()):
                    transposes(0, g)
                if i >= BANKS:
                    pe.wait_ge(found_ready, i - 1)
                look_up(i, i % 2, found_bank(i))

            def product_set(t, r):
                if r >= 2:
                    pe.wait_ge(merged, 2 * (SETS * t + r - 1))
                elif t >= 1:
                    pe.wait_ge(merged, 2 * (SETS * (t - 1) + r + 3))
                for q in range(PER_SET):
                    four = slice(QUADS * (r * PER_SET + q), QUADS * (r * PER_SET + q + 1))
                    last = nc.tensor.matmul(
                        pG[r % 2][0:GRAM_ROWS, q, 0:QUADS * FIELDS].rearrange("p (s f) -> p s f", s=QUADS),
                        CT[t % 2][:, :, :].rearrange("p s f -> p (s f)")[:, four.start * PAD:four.stop * PAD - (PAD - FIELDS)], CT[t % 2][:, four, 0:FIELDS],
                        start=True, stop=True)
                last.then_inc(gram, 1)

            def layer1_dense(t, m):
                nc.tensor.matmul(layer1_block(t, m), w1s[:, m * P:(m + 1) * P], xT[:, t * P:(t + 1) * P],
                                 start=True, stop=False)

            def layer1_pairs(t, m):
                pe.wait_ge(z_dve, MOVES * (t + 1))
                pe.wait_ge(z_act, MOVES * (t + 1))
                for k in range(KZ):
                    used = PAD * min(BLOCKS - QUADS * k, QUADS)
                    last = nc.tensor.matmul(layer1_block(t, m), w1z[0:used, k, m * P:(m + 1) * P], Z[t % 2][0:used, k, :],
                                            start=False, stop=(k == KZ - 1))
                if m % 2:
                    last.then_inc(h1_ps, 1)

            def layer1(t, *blocks):
                if t == 0:
                    pe.wait_ge(found_ready, NOH)
                    pe.wait_ge(wz_in, 16 * WZ)
                    pe.wait_ge(w1s_ready, 1)
                if t >= 1 and 0 in blocks:
                    pe.wait_ge(y_ready, t)
                for m in blocks:
                    layer1_dense(t, m)
                    layer1_pairs(t, m)

            def layer2(t):
                if t == 0:
                    pe.wait_ge(w2_in, 16)
                    pe.wait_ge(small_in, 16 * SMALL)
                if t < TILES - 1:
                    pe.wait_ge(h1_act, t + 1)
                for k0, ready in ((0, h1_dve), (2, h1_act)):
                    pe.wait_ge(ready, t + 1)
                    for m in range(M2):
                        for k in (k0, k0 + 1):
                            last = nc.tensor.matmul(pH[m][:, 2, :], w2_sb[:, k, m * P:(m + 1) * P], h1[t % 2][:, k, :],
                                                    start=(k == 0), stop=(k == M1 - 1))
                        if k0:
                            last.then_inc(h2_ps, 1)

            def layer3(t):
                for k, ready in enumerate((h2_dve, h2_act)):
                    pe.wait_ge(ready, t + 1)
                    last = nc.tensor.matmul(pY, w3_sb[:, k:k + 1], h2[:, k, :], start=(k == 0), stop=(k == M2 - 1))
                last.then_inc(y_ps, 1)

            for t in range(TILES):
                def next_tile(*groups):
                    if t + 1 < TILES:
                        for i in groups:
                            transposes(t + 1, i)

                if t == 0:
                    next_tile(0, 1)
                pe.wait_ge(ct_fixed, FIXED * (t + 1) if t else 2 * FIXED - 1)
                if t == 1:
                    pe.wait_ge(ct_zero, 2)
                pe.wait_ge(ct_dve, HALF * (t + 1))
                pe.wait_ge(ct_act, HALF * (t + 1))
                if t == 0:
                    pe.wait_ge(found_ready, 4)
                product_set(t, 0)
                if 2 <= t < TILES - 1:
                    layer3(t - 2)
                product_set(t, 1)
                if t == 0:
                    next_tile(2, 3)
                    product_set(t, 2)
                    next_tile(4, 5)
                    product_set(t, 3)
                    continue
                next_tile(0)
                if t < TILES - 1:
                    layer1(t - 1, 0, 1)
                product_set(t, 2)
                if t == TILES - 1:
                    break
                next_tile(1)
                layer1(t - 1, 2, 3)
                next_tile(2)
                if t < TILES - 2:
                    next_tile(3)
                    product_set(t, 3)
                    next_tile(4)
                    layer2(t - 1)
                    next_tile(5)
                else:
                    product_set(t, 3)
                    layer2(t - 1)
                    next_tile(3)
                    layer3(t - 1)
                    layer1(t, 2, 3)
                    next_tile(4)
                    layer1(t, 0)
                    next_tile(5)
                    layer1(t, 1)
            product_set(TILES - 1, 3)
            layer2(TILES - 2)
            pe.wait_ge(merged, 2 * (SETS * TILES - 1))
            pe.wait_ge(ct_dve, HALF * TILES)
            pe.wait_ge(ct_act, HALF * TILES)
            for m in range(M1):
                layer1_dense(TILES - 1, m)
            for m in (0, 1):
                layer1_pairs(TILES - 1, m)
            layer3(TILES - 2)
            for m in (2, 3):
                layer1_pairs(TILES - 1, m)
            pe.wait_ge(y_ready, TILES - 1)
            layer2(TILES - 1)
            layer3(TILES - 1)

        def row_numbers(copy, ks):
            return copy(row_h[:, ks, :], row_i[:, ks, None].to_broadcast([PT, ks.stop - ks.start, BATCH]))

        @block.scalar
        def _(act):
            def copy(dst, src):
                return nc.scalar.copy(dst, src)

            def fixed_field(t, f, source):
                column = CT[t % 2][:, :, f:f + 1].rearrange("p b f -> p (b f)")
                copy(column, source[:, t * P:(t + 1) * P]).then_inc(ct_fixed, 1)

            def fixed_fields(t):
                act.wait_ge(gram, SETS * (t - 1))
                fixed_field(t, 0, xT)
                for i, f in enumerate(ONEHOT):
                    fixed_field(t, f, found[:, i, :])

            def group(t, i):
                act.wait_ge(transposed, NG * t + i + 1)
                evacuate_group(copy, t, i, ct_act)

            def base_columns(t, r):
                act.wait_ge(gram, SETS * t + r + 1)
                if t >= 1 and r % (SETS // MOVES) == 0:
                    act.wait_ge(z_dve, MOVES * (t - 1) + r // (SETS // MOVES) + 1)
                for samples in HALVES:
                    for s in samples:
                        last = copy(merged_columns(r, s, BLOCKS), table_columns(r, s, SHIFT, BLOCKS))
                    last.then_inc(copied, 1)

            def move(t, part):
                act.wait_ge(merged, 2 * (SETS * t + (part + 1) * (SETS // MOVES)) - 1)
                move_merged(copy, HALVES[0], t, part, z_act)

            def hidden1(t):
                if t == 0:
                    act.wait_ge(small_in, 16 * SMALL)
                act.wait_ge(h1_ps, halves_done(t, 1))
                for m in (2, 3):
                    last = nc.scalar.activation(h1[t % 2][:, m, :], layer1_block(t, m), ACT.Relu, bias=b1_sb[:, m:m + 1])
                last.then_inc(h1_act, 1)

            def hidden2(t):
                act.wait_ge(h2_ps, M2 * (t + 1))
                nc.scalar.activation(h2[:, 1, :], pH[1][:, 2, :], ACT.Relu, bias=b2_sb[:, 1:2]).then_inc(h2_act, 1)

            act.wait_ge(row_i_ready, 1)
            row_numbers(copy, slice(0, KT // 2)).then_inc(row_h_ready, 1)
            def convert_ids(i):
                act.wait_ge(idw_in[i], 16)
                if i >= IDW:
                    act.wait_ge(direct_ready, i - IDW + 1)
                copy(idh[:, i % IDW, :], idw[0:PT, i % IDW, :]).then_inc(idh_ready, 1)

            def round_table(i):
                act.wait_ge(tab_in[i], 32)
                if i >= 2:
                    act.wait_ge(found_ps, i - 1)
                copy(high[:, i % 2, :], tab[:, i, :]).then_inc(high_ready, 1)

            def widen(i):
                act.wait_ge(staged_ready, i + 1)
                if i >= 2:
                    act.wait_ge(found_ps, i - 1)
                n = STAGED[i % 2]
                copy(onehot[:, i % 2, 0:n, :], staged[:, i % 2, 0:n, :]).then_inc(widened, 1)

            def rows_found(i):
                act.wait_ge(found_ps, i + 1)
                fixed_field(0, ONEHOT[i], found_bank(i))
                copy(found[:, i, P:BATCH], found_bank(i)[:, P:BATCH]).then_inc(found_ready, 1)

            convert_ids(0)
            act.wait_ge(ct_zero, 1)
            act.wait_ge(zero_ready, 1)
            copy(w1z[:, :, :], zero[:, None, :].to_broadcast([P, KZ, HID1])).then_inc(w1z_zero, 1)
            for i in range(NOH):
                if i == 0:
                    widen(i)
                if i >= 2:
                    rows_found(i - 2)
                round_table(i)
                if i + 1 < NOH:
                    convert_ids(i + 1)
                if i > 0:
                    widen(i)
                if i == 0:
                    act.wait_ge(xT_ps, 1)
                    copy(xT[:, :], pT[1][:, :, :].rearrange("p t b -> p (t b)")).then_inc(xT_ready, 1)
                if i == 1:
                    act.wait_ge(xT_ready, 1)
                    fixed_field(0, 0, xT)
                for g in FIRST_GROUPS.get(i, ()):
                    if g % 2:
                        group(0, g)
            rows_found(NOH - 2)
            fixed_field(1, 0, xT)
            act.wait_ge(found_ready, NOH - 1)
            for i, f in enumerate(ONEHOT[:-1]):
                fixed_field(1, f, found[:, i, :])
            rows_found(NOH - 1)
            for t in range(TILES):
                if t == 0:
                    act.wait_ge(z_zero, 2)
                    group(1, 1)
                base_columns(t, 0)
                base_columns(t, 1)
                if t == 0:
                    act.wait_ge(found_ready, NOH)
                    fixed_field(1, ONEHOT[-1], found[:, NOH - 1, :])
                    group(1, 3)
                    base_columns(t, 2)
                    group(1, 5)
                    move(t, 0)
                    base_columns(t, 3)
                    move(t, 1)
                    continue
                if t + 1 < TILES:
                    fixed_fields(t + 1)
                move(t, 0)
                base_columns(t, 2)
                if t == TILES - 1:
                    break
                group(t + 1, 1)
                hidden1(t - 1)
                if t < TILES - 2:
                    group(t + 1, 3)
                    base_columns(t, 3)
                    group(t + 1, 5)
                    move(t, 1)
                    hidden2(t - 1)
                else:
                    base_columns(t, 3)
                    move(t, 1)
                    hidden2(t - 1)
                    group(t + 1, 3)
                    hidden1(t)
                    group(t + 1, 5)
            base_columns(TILES - 1, 3)
            move(TILES - 1, 1)
            hidden2(TILES - 2)
            hidden1(TILES - 1)
            hidden2(TILES - 1)

        @block.vector
        def _(dve):
            def copy(dst, src):
                return nc.vector.tensor_copy(dst, src)

            def copy_one_port(dst, src):
                return nc.vector.tensor_tensor(dst, src, src, ALU.max)

            def group(t, i):
                dve.wait_ge(transposed, NG * t + i + 1)
                evacuate_group(copy, t, i, ct_dve)

            def merge(t, r):
                for half, samples in enumerate(HALVES):
                    dve.wait_ge(copied, 2 * (SETS * t + r) + half + 1)
                    for s in samples:
                        out_cols = merged_columns(r, s, SHIFT)
                        keep = mask[used_rows(s), None, :].to_broadcast(list(out_cols.shape))
                        last = nc.vector.copy_predicated(out_cols, keep, table_columns(r, s, 0, SHIFT))
                    last.then_inc(merged, 1)

            def move(t, part):
                dve.wait_ge(merged, 2 * (SETS * t + (part + 1) * (SETS // MOVES)))
                move_merged(copy if t == TILES - 1 else copy_one_port, HALVES[1], t, part, z_dve)

            def hidden1(t):
                if t == 0:
                    dve.wait_ge(small_in, 16 * SMALL)
                dve.wait_ge(h1_ps, halves_done(t, 0))
                for m in (0, 1):
                    last = nc.vector.tensor_scalar(h1[t % 2][:, m, :], layer1_block(t, m), b1_sb[:, m:m + 1], 0.0,
                                                   ALU.add, ALU.max)
                last.then_inc(h1_dve, 1)

            def hidden2(t):
                dve.wait_ge(h2_ps, M2 * t + 1)
                nc.vector.tensor_scalar(h2[:, 0, :], pH[0][:, 2, :], b2_sb[:, 0:1], 0.0,
                                        ALU.add, ALU.max).then_inc(h2_dve, 1)

            def result(t):
                dve.wait_ge(y_ps, t + 1)
                nc.vector.tensor_copy(y[:, bass.ds(t * P, P)], pY).then_inc(y_ready, 1)

            def one_hot(out, i, ks):
                return nc.vector.tensor_tensor(out, row_h[:, ks, :],
                                               idh[:, i % IDW, None, :].to_broadcast([PT, ks.stop - ks.start, BATCH]), ALU.is_equal)

            dve.wait_ge(row_i_ready, 1)
            row_numbers(copy, slice(KT // 2, KT)).then_inc(row_h_ready, 1)
            nc.vector.memset(CT[0][:, :, FIELDS:PAD], 0.0).then_inc(ct_zero, 1)
            dve.wait_ge(row_h_ready, 2)
            for i in range(NOH):
                dve.wait_ge(idh_ready, i + 1)
                if i >= 2:
                    dve.wait_ge(widened, i - 1)
                n = STAGED[i % 2]
                one_hot(staged[:, i % 2, 0:n, :], i, slice(0, n)).then_inc(staged_ready, 1)
                if i >= 2:
                    dve.wait_ge(found_ps, i - 1)
                one_hot(onehot[:, i % 2, n:KT, :], i, slice(n, KT)).then_inc(direct_ready, 1)
                dve.wait_ge(tab_in[i], 32)
                dve.wait_ge(high_ready, i + 1)
                nc.vector.tensor_tensor(low[:, i % 2, :], tab[:, i, :], high[:, i % 2, :].bitcast(fp32),
                                        ALU.subtract).then_inc(low_ready, 1)
                for g in FIRST_GROUPS.get(i, ()):
                    if g % 2 == 0:
                        group(0, g)
            dve.wait_ge(behind_ready, 1)
            nc.vector.tensor_scalar(after[:, :], behind[:, :], 1, None, ALU.is_ge).then_inc(after_ready, 1)
            dve.wait_ge(after_ready, 1)
            nc.vector.scalar_tensor_tensor(mask[:, :], behind[:, :], SHIFT, after[:, :],
                                           ALU.is_le, ALU.mult).then_inc(mask_ready, 1)
            nc.vector.memset(CT[1][:, :, FIELDS:PAD], 0.0).then_inc(ct_zero, 1)
            dve.wait_ge(wx_in, 32)
            nc.vector.tensor_tensor(w1s[:, :], w1x[:, 0, :], w1x[:, 1, :], ALU.add).then_inc(w1s_ready, 1)
            dve.wait_ge(mask_ready, 1)
            for t in range(TILES):
                if t == 0:
                    dve.wait_ge(z_zero, 2)
                    group(1, 0)
                merge(t, 0)
                if 2 <= t < TILES - 1:
                    result(t - 2)
                merge(t, 1)
                if t == 0:
                    group(1, 2)
                    move(t, 0)
                    merge(t, 2)
                    group(1, 4)
                    merge(t, 3)
                    move(t, 1)
                    continue
                move(t, 0)
                if t + 1 < TILES:
                    group(t + 1, 0)
                if 1 <= t < TILES - 1:
                    hidden1(t - 1)
                merge(t, 2)
                if t + 1 < TILES:
                    group(t + 1, 2)
                merge(t, 3)
                if t == TILES - 1:
                    break
                if t < TILES - 2:
                    group(t + 1, 4)
                    move(t, 1)
                    if t >= 1:
                        hidden2(t - 1)
                else:
                    hidden2(t - 1)
                    move(t, 1)
                    result(t - 1)
                    group(t + 1, 4)
                    hidden1(t)
            move(TILES - 1, 1)
            hidden2(TILES - 2)
            hidden1(TILES - 1)
            result(TILES - 2)
            hidden2(TILES - 1)
            result(TILES - 1)



_INS = (["r_dense_output", "ids", "ids_by_table"] + [f"tbl_{i}" for i in range(TABLES)]
        + ["W_top1", "b_top1", "W_top2", "b_top2", "W_top3"])


def kernel(**inputs):
    import numpy as _np
    import concourse.bacc as _bacc
    from concourse import mybir as _mybir
    from concourse.bass_utils import run_bass_kernel_spmd as _run

    nc = _bacc.Bacc("TRN2", target_bir_lowering=False, num_devices=1)
    arrays, args = {}, []
    inputs["ids_by_table"] = _np.asarray(inputs["ids"]).T
    for name in _INS:
        a = _np.ascontiguousarray(inputs[name])
        arrays[f"in_{name}_dram"] = a
        args.append(nc.dram_tensor(f"in_{name}_dram", a.shape, _mybir.dt.from_np(a.dtype), kind="ExternalInput").ap())
    out = nc.dram_tensor("out_0_dram", (BATCH, 1), _mybir.dt.float32, kind="ExternalOutput").ap()
    dlrm_tower(nc, *args[:3], args[3:3 + TABLES], *args[3 + TABLES:], out)
    r = _run(nc, [arrays], core_ids=[0])
    return r.results[0]["out_0_dram"]
```
